# Optimizing a Trainium2 kernel written in Bass

```python
import numpy as np
import jax
import jax.numpy as jnp

def _softmax(x, axis=-1):
    return jax.nn.softmax(x, axis=axis)

def _gelu(x):
    return jax.nn.gelu(x, approximate=True)

def _silu(x):
    return jax.nn.silu(x)

def _sigmoid(x):
    return jax.nn.sigmoid(x)

def _layernorm(x, axis=-1, eps=1e-05):
    m = jnp.mean(x, axis=axis, keepdims=True)
    v = jnp.var(x, axis=axis, keepdims=True)
    return (x - m) / jnp.sqrt(v + eps)

def _scatter_add(tgt, idx, src, axis=0):
    return tgt.at[idx].add(src)

def _segment_sum(src, seg, n):
    return jax.ops.segment_sum(src, seg, n)
kernel_name = 'mk_rec_standalone_d1_rec_r8_df5cf2'

def setup_inputs(seed: int=0):
    np.random.seed(seed)
    _w = jnp.asarray

    def _rec_inputs():
        import jax
        import jax.numpy as jnp
        _rk = jax.random.key(seed)
        r_query = 0.00191187 + 0.999416 * jax.random.normal(jax.random.fold_in(_rk, 1), (2048, 64), jnp.float32)
        r_keys = -8.015e-05 + 0.999903 * jax.random.normal(jax.random.fold_in(_rk, 2), (2048, 200, 64), jnp.float32)
        r_seq_len = jax.random.randint(jax.random.fold_in(_rk, 3), (2048,), 0, 200, jnp.int32)
        return (r_query, r_keys, r_seq_len)
    r_query, r_keys, r_seq_len = _rec_inputs()

    def _L0_rec_setup():
        import jax, jax.numpy as jnp
        import numpy as np
        B, T, E = (512, 200, 64)
        HIDDEN = [80, 40]
        MASK_VAL = jnp.float32(-2.0 ** 32 + 1)
        key = jax.random.key(seed)
        ks = jax.random.split(key, 10)
        keys = jax.random.normal(ks[0], (B, T, E), dtype=jnp.float32)
        query = jax.random.normal(ks[1], (B, E), dtype=jnp.float32)
        seq_len = jax.random.randint(ks[2], (B,), 0, T, dtype=jnp.int32)
        d_in = 4 * E
        dims = [d_in] + HIDDEN + [1]
        W1 = jax.random.normal(ks[3], (dims[0], dims[1]), dtype=jnp.float32) / np.sqrt(dims[0])
        b1 = jnp.zeros((dims[1],), dtype=jnp.float32)
        W2 = jax.random.normal(ks[4], (dims[1], dims[2]), dtype=jnp.float32) / np.sqrt(dims[1])
        b2 = jnp.zeros((dims[2],), dtype=jnp.float32)
        W3 = jax.random.normal(ks[5], (dims[2], dims[3]), dtype=jnp.float32) / np.sqrt(dims[2])
        b3 = jnp.zeros((dims[3],), dtype=jnp.float32)
        return {'keys': keys, 'query': query, 'seq_len': seq_len, 'W1': W1, 'b1': b1, 'W2': W2, 'b2': b2, 'W3': W3, 'b3': b3}
    _L0_rec_all = _L0_rec_setup()
    _L0_rec_in = {k: v for k, v in _L0_rec_all.items() if k in ('W1', 'b1', 'W2', 'b2', 'W3', 'b3')}
    del _L0_rec_all
    return {'r_query': r_query, 'r_keys': r_keys, 'r_seq_len': r_seq_len, 'L0_rec_W1': _L0_rec_in['W1'], 'L0_rec_b1': _L0_rec_in['b1'], 'L0_rec_W2': _L0_rec_in['W2'], 'L0_rec_b2': _L0_rec_in['b2'], 'L0_rec_W3': _L0_rec_in['W3'], 'L0_rec_b3': _L0_rec_in['b3']}

def reference(r_query, r_keys, r_seq_len, L0_rec_W1, L0_rec_b1, L0_rec_W2, L0_rec_b2, L0_rec_W3, L0_rec_b3):
    import jax
    import jax.numpy as jnp

    def _L0_rec_ref(keys, query, seq_len, W1, b1, W2, b2, W3, b3):
        import jax, jax.numpy as jnp
        import numpy as np
        B, T, E = (512, 200, 64)
        HIDDEN = [80, 40]
        MASK_VAL = jnp.float32(-2.0 ** 32 + 1)
        q = jnp.broadcast_to(query[:, None, :], keys.shape)
        din_all = jnp.concatenate([q, keys, q - keys, q * keys], axis=-1)
        h = jax.nn.relu(jnp.einsum('btd,dh->bth', din_all, W1) + b1)
        h = jax.nn.relu(jnp.einsum('btd,dh->bth', h, W2) + b2)
        logits = jnp.einsum('btd,dh->bth', h, W3) + b3
        scores = jnp.transpose(logits, (0, 2, 1))
        mask = (jnp.arange(T)[None, :] < seq_len[:, None])[:, None, :]
        scores = jnp.where(mask, scores, MASK_VAL)
        scores = jax.nn.softmax(scores, axis=-1)
        out = jnp.squeeze(jnp.matmul(scores, keys), axis=1)
        return jnp.concatenate([out, query], axis=-1)
    y = _L0_rec_ref(r_keys, r_query, r_seq_len, L0_rec_W1, L0_rec_b1, L0_rec_W2, L0_rec_b2, L0_rec_W3, L0_rec_b3)
    return y

_drawn_inputs = setup_inputs


def setup_inputs(seed=0):
    import zlib

    import numpy as np

    out = dict(_drawn_inputs(seed))
    spreads = {'L0_rec_b1': (0.0, 0.8), 'L0_rec_b2': (0.0, 0.8)}
    factors = {}
    for name, (base, spread) in spreads.items():
        noise = np.random.default_rng([zlib.crc32(name.encode()), seed]).standard_normal(out[name].shape)
        drawn = base * np.exp(spread * noise) if base else spread * noise
        out[name] = jnp.asarray(drawn.astype(out[name].dtype))
    for name, factor in factors.items():
        out[name] = (out[name] * factor).astype(out[name].dtype)
    return out
```

```python
import concourse.bass as bass
from concourse import mybir
from contextlib import ExitStack

FP32 = mybir.dt.float32
INT32 = mybir.dt.int32
ALU = mybir.AluOpType
ACT = mybir.ActivationFunctionType
AXIS = mybir.AxisListType

B, T, E = 2048, 200, 64
H1, H2 = 80, 40
HEAD, TAIL = 64, H1 - 64
PAIRS, OCTETS = 4, 4
GROUPS = B // (2 * PAIRS * OCTETS)
HALF = T // 2
ROWS = 2 * OCTETS
QUAD = 32
K2 = HEAD + QUAD
WCOLS = 2 * HEAD + QUAD
PARAMS = 2 * PAIRS + 1
MASKED = -2.0 ** 32

W1_AT, W2_AT = 0, 4 * WCOLS
W3_AT = W2_AT + 2 * 64
BIAS_AT = W3_AT + OCTETS * QUAD
WEIGHTS = BIAS_AT + 4
IDENT_AT, IOTA_AT = 0, 128
OWN_AT = IOTA_AT + T
CONSTS = OWN_AT + ROWS * E


def build(nc, keys_t, keys_n, query_t, query_n, lengths, weights, consts, out):
    ctx = ExitStack()
    with ctx:
        def sbuf(name, shape, dtype=FP32):
            return ctx.enter_context(nc.sbuf_tensor(name, shape, dtype))

        def psum(name):
            return ctx.enter_context(nc.psum_tensor(name, [128, 512], FP32))

        def sem(name):
            return ctx.enter_context(nc.semaphore(name))

        key_t = sbuf("key_t", [128, OCTETS, PAIRS, T])
        key_n = sbuf("key_n", [HALF, 2, PAIRS, ROWS * E])
        h1 = sbuf("h1", [K2, 2, PAIRS, 2, T])
        h2 = sbuf("h2", [128, 2, PAIRS, T])
        w = sbuf("w", [128, WEIGHTS])
        c = sbuf("c", [128, CONSTS])
        w_key = sbuf("w_key", [128, WCOLS])
        w_query = sbuf("w_query", [128, WCOLS])
        q_all = sbuf("q_all", [128, GROUPS * OCTETS, PAIRS])
        params = sbuf("params", [128, GROUPS * OCTETS, PARAMS])
        own = sbuf("own", [128, OCTETS, PARAMS])
        w_own = sbuf("w_own", [128, 2, PAIRS, WCOLS])
        w_scaled = sbuf("w_scaled", [128, PAIRS, WCOLS])
        len_i = sbuf("len_i", [128, GROUPS], INT32)
        len_f = sbuf("len_f", [128, GROUPS])
        valid = sbuf("valid", [128, T])
        penalty = sbuf("penalty", [128, T])
        kept = sbuf("kept", [128, T])
        score = sbuf("score", [128, T])
        top = sbuf("top", [128, 1])
        neg_top = sbuf("neg_top", [128, 1])
        prob = sbuf("prob", [128, T])
        total = sbuf("total", [128, 1])
        inv_total = sbuf("inv_total", [128, 1])
        prob_t = sbuf("prob_t", [HALF, 2, 128])
        pooled_all = sbuf("pooled_all", [128, ROWS, E])
        pooled = sbuf("pooled", [128, E])

        w1d = w[:, W1_AT + 3 * WCOLS:W1_AT + 4 * WCOLS]
        w2 = w[:, W2_AT:W3_AT].rearrange("p (s j) -> p s j", s=2)
        w3 = w[:, W3_AT:BIAS_AT].rearrange("p (o j) -> p o j", o=OCTETS)
        b1_head, b1_tail, b2_col, b3_col = (w[:, BIAS_AT + n:BIAS_AT + n + 1] for n in range(4))
        ident = c[:, IDENT_AT:IOTA_AT]
        iota = c[:, IOTA_AT:OWN_AT]
        own_block = c[:, OWN_AT:CONSTS]

        head_ps = [psum(f"head{n}") for n in range(2)]
        tail_ps = psum("tail")
        h2_ps = [psum(f"h2_{n}") for n in range(2)]
        logit_ps = psum("logit")
        prob_t_ps = psum("prob_t_ps")
        out_ps = psum("out_ps")

        weights_in = sem("weights_in")
        consts_in = sem("consts_in")
        query_in = sem("query_in")
        lengths_in = sem("lengths_in")
        lengths_clear = sem("lengths_clear")
        lengths_ready = sem("lengths_ready")
        w1_ready = sem("w1_ready")
        bias_done = sem("bias_done")
        params_ready = sem("params_ready")
        key_t_in = [sem(f"key_t_in{o}") for o in range(OCTETS)]
        key_n_in = sem("key_n_in")
        own_step = sem("own_step")
        mask_step = sem("mask_step")
        head_done = sem("head_done")
        tail_done = sem("tail_done")
        h1_act = sem("h1_act")
        h1_dve = sem("h1_dve")
        h2_done = sem("h2_done")
        h2_ready = sem("h2_ready")
        logit_done = sem("logit_done")
        soft_step = sem("soft_step")
        prob_ready = sem("prob_ready")
        prob_t_done = sem("prob_t_done")
        prob_t_ready = sem("prob_t_ready")
        out_done = sem("out_done")
        pool_step = sem("pool_step")
        inv_ready = sem("inv_ready")
        stored = sem("stored")

        SOFT, POOL, OWN, MASK = 4, 3, 3, 2

        def wait(eng, semaphore, value):
            if not isinstance(value, int) or value > 0:
                eng.wait_ge(semaphore, value)

        block = ctx.enter_context(nc.Block())


        @block.sync
        def _(sp):
            def load_key_t(g, o):
                sp.dma_start(key_t[:, o], keys_t[g]).then_inc(key_t_in[o], 16)

            def load_key_n(i):
                sp.dma_start(key_n[0:96], keys_n[i, 0:96]).then_inc(key_n_in, 16)
                sp.dma_start(key_n[96:HALF], keys_n[i, 96:HALF]).then_inc(key_n_in, 16)

            def store(i):
                sp.wait_ge(pool_step, POOL * (i + 1))
                for q in range(PAIRS):
                    sp.dma_start(out[i, q, :, 0:E], pooled[QUAD * q:QUAD * q + ROWS]).then_inc(stored, 16)

            sp.dma_start(w[:], weights).then_inc(weights_in, 16)
            sp.dma_start(q_all[:], query_t).then_inc(query_in, 16)
            load_key_t(0, 0)
            sp.dma_start(c[:], consts).then_inc(consts_in, 16)
            sp.wait_ge(lengths_clear, 1)
            for q in range(PAIRS):
                sp.dma_start(len_i[QUAD * q:QUAD * q + ROWS], lengths[q]).then_inc(lengths_in, 16)
            for o in range(1, OCTETS):
                load_key_t(o, o)
            load_key_n(0)
            sp.dma_start(out[:, :, :, E:2 * E], query_n).then_inc(stored, 16)

            def body(i, first):
                for o in range(OCTETS):
                    sp.wait_ge(tail_done, 4 * i + o + 1)
                    load_key_t(4 * i + 4 + o, o)
                    if o == 0 and not first:
                        store(i - 2)
                if not first:
                    sp.wait_ge(out_done, i)
                    load_key_n(i)

            body(0, True)
            for o in range(OCTETS):
                sp.wait_ge(tail_done, 4 + o + 1)
                load_key_t(8 + o, o)
            sp.wait_ge(out_done, 1)
            load_key_n(1)
            with sp.Fori(2, GROUPS - 1) as i:
                body(i, False)
            store(GROUPS - 3)
            sp.wait_ge(out_done, GROUPS - 1)
            load_key_n(GROUPS - 1)
            store(GROUPS - 2)
            store(GROUPS - 1)
            sp.wait_ge(stored, 16 * (PAIRS * GROUPS + 1))

        @block.gpsimd
        def _(pool):
            nc.gpsimd.memset(len_i[:], 0).then_inc(lengths_clear, 1)
            pool.wait_ge(lengths_in, 16 * PAIRS)
            nc.gpsimd.tensor_copy(len_f[:], len_i[:]).then_inc(lengths_ready, 1)
            pool.wait_ge(w1_ready, 2)
            pool.wait_ge(params_ready, 4)

            def octet_weights(g, o):
                wait(pool, tail_done, g - 1)
                nc.gpsimd.tensor_copy(own[:, o], params[:, g]).then_inc(own_step, 1)
                pool.wait_ge(own_step, OWN * g + 1)
                shape = [128, PAIRS, WCOLS]
                nc.gpsimd.tensor_tensor(
                    w_scaled[:], w1d[:, None, :].broadcast_to(shape),
                    own[:, o, 0:PAIRS, None].broadcast_to(shape), ALU.mult).then_inc(own_step, 1)
                pool.wait_ge(own_step, OWN * g + 2)
                nc.gpsimd.tensor_tensor(
                    w_own[:, o % 2], w_scaled[:], w_key[:, None, :].broadcast_to(shape),
                    ALU.add).then_inc(own_step, 1)

            def body(i, first):
                for o in range(OCTETS):
                    octet_weights(4 * i + o, o)

            body(0, True)
            with pool.Fori(1, GROUPS) as i:
                body(i, False)

        @block.tensor
        def _(pe):
            pe.wait_ge(w1_ready, 2)
            pe.wait_ge(query_in, 16)
            half = GROUPS * OCTETS // 2
            for n in range(2):
                nc.tensor.matmul(head_ps[n][:, :], w_query[:, 0:2 * HEAD],
                                 q_all[:, n * half:(n + 1) * half].rearrange("p g n -> p (g n)"),
                                 start=True, stop=True).then_inc(bias_done, 1)
            for p in range(PAIRS):
                last = nc.tensor.matmul(tail_ps[QUAD * p:QUAD * (p + 1), 0:GROUPS * OCTETS],
                                        w_query[:, 2 * HEAD:WCOLS], q_all[:, :, p],
                                        start=True, stop=True)
            last.then_inc(bias_done, 1)
            pe.wait_ge(params_ready, 4)

            def layer1_heads(i, g, o):
                pe.wait_ge(key_t_in[o], 16 * (i + 1))
                pe.wait_ge(own_step, OWN * (g + 1))
                for n in range(2):
                    wait(pe, h1_act, 3 * (g - 1) + n + 1)
                    wait(pe, h1_dve, 3 * (g - 1) + n + 1)
                    for p in (2 * n, 2 * n + 1):
                        last = nc.tensor.matmul(head_ps[n][:, T * (p % 2):T * (p % 2 + 1)],
                                                w_own[:, o % 2, p, 0:2 * HEAD], key_t[:, o, p],
                                                start=True, stop=True)
                    last.then_inc(head_done, 1)

            def layer1_tails(g, o):
                wait(pe, h1_act, 3 * g)
                wait(pe, h1_dve, 3 * g)
                for p in range(PAIRS):
                    last = nc.tensor.matmul(tail_ps[QUAD * p:QUAD * (p + 1), 0:T],
                                            w_own[:, o % 2, p, 2 * HEAD:WCOLS], key_t[:, o, p],
                                            start=True, stop=True)
                last.then_inc(tail_done, 1)

            def layer2(g, o):
                pe.wait_ge(h1_act, 3 * (g + 1))
                pe.wait_ge(h1_dve, 3 * (g + 1))
                for n in range(2):
                    wait(pe, h2_ready, 2 * (g - 1) + n + 1)
                    for p in (2 * n, 2 * n + 1):
                        for s in range(2):
                            last = nc.tensor.matmul(
                                h2_ps[n][64 * s:64 * (s + 1), T * (p % 2):T * (p % 2 + 1)],
                                w2[0:K2, s], h1[:, o % 2, p, s], start=True, stop=True)
                    last.then_inc(h2_done, 1)

            def layer3(i, g, o):
                pe.wait_ge(h2_ready, 2 * (g + 1))
                if o == 0:
                    wait(pe, soft_step, SOFT * (i - 1) + 1)
                for p in range(PAIRS):
                    last = nc.tensor.matmul(logit_ps[QUAD * p:QUAD * (p + 1), 0:T], w3[:, o],
                                            h2[:, o % 2, p], start=o == 0, stop=o == OCTETS - 1)
                last.then_inc(logit_done, 1)

            def turn_probs(i):
                pe.wait_ge(prob_ready, i + 1)
                wait(pe, prob_t_ready, i)
                for n in range(2):
                    last = nc.tensor.transpose(prob_t_ps[0:HALF, 128 * n:128 * (n + 1)],
                                               prob[:, HALF * n:HALF * (n + 1)], ident)
                last.then_inc(prob_t_done, 1)

            def pool_keys(i):
                pe.wait_ge(prob_t_ready, i + 1)
                pe.wait_ge(key_n_in, 32 * (i + 1))
                wait(pe, pool_step, POOL * (i - 1) + 1)
                for n in range(2):
                    for q in range(PAIRS):
                        last = nc.tensor.matmul(out_ps[QUAD * q:QUAD * (q + 1), 0:ROWS * E],
                                                prob_t[:, n, QUAD * q:QUAD * (q + 1)], key_n[:, n, q],
                                                start=n == 0, stop=n == 1)
                last.then_inc(out_done, 1)

            def body(i, first):
                for o in range(OCTETS):
                    g = 4 * i + o
                    layer1_heads(i, g, o)
                    layer1_tails(g, o)
                    if o >= 2 or not first:
                        j = i if o >= 2 else i - 1
                        layer3(j, g - 2, (o - 2) % 4)
                    if o == 3 and not first:
                        pool_keys(i - 1)
                    if o >= 1 or not first:
                        layer2(g - 1, (o - 1) % 4)
                    if o == 2 and not first:
                        turn_probs(i - 1)

            body(0, True)
            body(1, False)
            with pe.Fori(2, GROUPS) as i:
                body(i, False)
            i, g = GROUPS - 1, 4 * GROUPS
            layer3(i, g - 2, 2)
            layer2(g - 1, 3)
            layer3(i, g - 1, 3)
            turn_probs(i)
            pool_keys(i)

        @block.scalar
        def _(act):
            def heads_of_first(g, o):
                for p in range(PAIRS):
                    if p % 2 == 0:
                        act.wait_ge(head_done, 2 * g + p // 2 + 1)
                    last = nc.scalar.activation(
                        h1[0:HEAD, o % 2, p, 0], head_ps[p // 2][0:HEAD, T * (p % 2):T * (p % 2 + 1)],
                        ACT.Relu, bias=own[0:HEAD, o, PAIRS + p:PAIRS + p + 1])
                    if p % 2:
                        last.then_inc(h1_act, 1)

            def tails(g, o):
                act.wait_ge(tail_done, g + 1)
                for p in (0, 1):
                    rows = slice(QUAD * p, QUAD * (p + 1))
                    last = nc.scalar.activation(
                        h1[HEAD:K2, o % 2, p],
                        tail_ps[rows, None, 0:T].broadcast_to([QUAD, 2, T]),
                        ACT.Relu, bias=own[rows, o, 2 * PAIRS:PARAMS])
                last.then_inc(h1_act, 1)

            def layer2_out(g, o):
                wait(act, logit_done, g - 1)
                for n in range(2):
                    act.wait_ge(h2_done, 2 * g + n + 1)
                    nc.scalar.activation(
                        h2[:, o % 2, 2 * n:2 * n + 2].rearrange("p a t -> p (a t)"),
                        h2_ps[n][:, 0:2 * T], ACT.Relu, bias=b2_col).then_inc(h2_ready, 1)

            def exponentials(i):
                act.wait_ge(soft_step, SOFT * (i + 1))
                wait(act, prob_t_done, i)
                wait(act, pool_step, POOL * (i - 1) + 1)
                nc.scalar.activation(prob[:], score[:], ACT.Exp, bias=neg_top[:, 0:1],
                                     accum_out=total[:, 0:1]).then_inc(prob_ready, 1)

            def body(i, first):
                for o in range(OCTETS):
                    g = 4 * i + o
                    if o >= 2 or not first:
                        layer2_out(g - 2, (o - 2) % 4)
                    if o == 2 and not first:
                        exponentials(i - 1)
                    heads_of_first(g, o)
                    tails(g, o)

            act.wait_ge(weights_in, 16)
            body(0, True)
            body(1, False)
            with act.Fori(2, GROUPS) as i:
                body(i, False)
            layer2_out(4 * GROUPS - 2, 2)
            layer2_out(4 * GROUPS - 1, 3)
            exponentials(GROUPS - 1)

        @block.vector
        def _(dve):
            dve.wait_ge(weights_in, 16)

            def w1(n):
                return w[:, W1_AT + n * WCOLS:W1_AT + (n + 1) * WCOLS]

            nc.vector.tensor_tensor(w_query[:], w1(0), w1(2), ALU.add).then_inc(w1_ready, 1)
            nc.vector.tensor_tensor(w_key[:], w1(1), w1(2), ALU.subtract).then_inc(w1_ready, 1)
            dve.wait_ge(query_in, 16)
            nc.vector.tensor_copy(params[:, :, 0:PAIRS], q_all[:]).then_inc(params_ready, 1)
            half = GROUPS * OCTETS // 2
            for n in range(2):
                dve.wait_ge(bias_done, n + 1)
                nc.vector.tensor_scalar(
                    params[:, n * half:(n + 1) * half, PAIRS:2 * PAIRS],
                    head_ps[n][:, :].rearrange("p (g n) -> p g n", n=PAIRS),
                    b1_head, None, ALU.add).then_inc(params_ready, 1)
            dve.wait_ge(bias_done, 3)
            nc.vector.tensor_scalar(params[:, :, 2 * PAIRS], tail_ps[:, 0:GROUPS * OCTETS],
                                    b1_tail, None, ALU.add).then_inc(params_ready, 1)

            def heads_of_second(g, o):
                wait(dve, h2_done, 2 * (g - 1))
                for p in range(PAIRS):
                    if p % 2 == 0:
                        dve.wait_ge(head_done, 2 * g + p // 2 + 1)
                    last = nc.vector.tensor_scalar(
                        h1[0:HEAD, o % 2, p, 1], head_ps[p // 2][HEAD:128, T * (p % 2):T * (p % 2 + 1)],
                        own[HEAD:128, o, PAIRS + p:PAIRS + p + 1], 0.0, ALU.add, ALU.max)
                    if p % 2:
                        last.then_inc(h1_dve, 1)

            def tails(g, o):
                dve.wait_ge(tail_done, g + 1)
                for p in (2, 3):
                    rows = slice(QUAD * p, QUAD * (p + 1))
                    last = nc.vector.tensor_scalar(
                        h1[HEAD:K2, o % 2, p],
                        tail_ps[rows, None, 0:T].broadcast_to([QUAD, 2, T]),
                        own[rows, o, 2 * PAIRS:PARAMS], 0.0, ALU.add, ALU.max)
                last.then_inc(h1_dve, 1)

            def masked_scores(i):
                length = len_f[:, bass.ds(i, 1)]
                nc.vector.tensor_scalar(valid[:], iota, length, None, ALU.is_lt).then_inc(mask_step, 1)
                nc.vector.tensor_scalar(penalty[:], iota, length, MASKED,
                                        ALU.is_ge, ALU.mult).then_inc(mask_step, 1)
                dve.wait_ge(logit_done, 4 * (i + 1))
                dve.wait_ge(mask_step, MASK * (i + 1))
                wait(dve, prob_ready, i)
                nc.vector.scalar_tensor_tensor(kept[:], logit_ps[:, 0:T], b3_col, valid[:],
                                               ALU.add, ALU.mult).then_inc(soft_step, 1)
                dve.wait_ge(soft_step, SOFT * i + 1)
                nc.vector.tensor_tensor(score[:], kept[:], penalty[:], ALU.add).then_inc(soft_step, 1)
                dve.wait_ge(soft_step, SOFT * i + 2)
                nc.vector.reduce_max(top[:], score[:], AXIS.X).then_inc(soft_step, 1)
                dve.wait_ge(soft_step, SOFT * i + 3)
                nc.vector.tensor_scalar(neg_top[:], top[:], -1.0, None, ALU.mult).then_inc(soft_step, 1)

            def probs_to_sbuf(i):
                dve.wait_ge(prob_t_done, i + 1)
                wait(dve, out_done, i)
                nc.vector.tensor_copy(prob_t[:].rearrange("p h n -> p (h n)"),
                                      prob_t_ps[0:HALF, 0:256]).then_inc(prob_t_ready, 1)

            def pooled_out(i):
                dve.wait_ge(out_done, i + 1)
                nc.vector.reciprocal(inv_total[:], total[:]).then_inc(inv_ready, 1)
                dve.wait_ge(inv_ready, i + 1)
                nc.vector.scalar_tensor_tensor(
                    pooled_all[:].rearrange("p r e -> p (r e)"), out_ps[:, :], inv_total[:, 0:1],
                    own_block, ALU.mult, ALU.mult).then_inc(pool_step, 1)
                dve.wait_ge(pool_step, POOL * i + 1)
                dve.wait_ge(stored, 16 * (PAIRS * i + 1))
                nc.vector.reduce_sum(pooled[:], pooled_all[:].rearrange("p r e -> p e r"),
                                     AXIS.X).then_inc(pool_step, 2)

            def body(i, first, second=False):
                for o in range(OCTETS):
                    g = 4 * i + o
                    if o == 3 and not first:
                        probs_to_sbuf(i - 1)
                    heads_of_second(g, o)
                    tails(g, o)
                    if o == 0 and not first and not second:
                        pooled_out(i - 2)
                    if o == 1 and not first:
                        masked_scores(i - 1)

            dve.wait_ge(lengths_ready, 1)
            dve.wait_ge(consts_in, 16)
            body(0, True)
            body(1, False, True)
            with dve.Fori(2, GROUPS) as i:
                body(i, False)
            pooled_out(GROUPS - 2)
            masked_scores(GROUPS - 1)
            probs_to_sbuf(GROUPS - 1)
            pooled_out(GROUPS - 1)


def kernel(r_query, r_keys, r_seq_len, L0_rec_W1, L0_rec_b1, L0_rec_W2, L0_rec_b2, L0_rec_W3, L0_rec_b3):
    import numpy as np
    import concourse.bacc as bacc
    from concourse.bass_utils import run_bass_kernel_spmd

    arrays = [np.asarray(x) for x in (r_query, r_keys, r_seq_len, L0_rec_W1, L0_rec_b1,
                                      L0_rec_W2, L0_rec_b2, L0_rec_W3, L0_rec_b3)]
    query, keys, length, W1, b1, W2, b2, W3, b3 = arrays

    keys_t = np.ascontiguousarray(
        keys.reshape(GROUPS * OCTETS, PAIRS, 2, T, E).transpose(0, 2, 4, 1, 3)
    ).reshape(GROUPS * OCTETS, 2 * E, PAIRS, T)
    keys_n = np.ascontiguousarray(
        keys.reshape(GROUPS, OCTETS, PAIRS, 2, 2, HALF, E).transpose(0, 5, 4, 2, 1, 3, 6)
    ).reshape(GROUPS, HALF, 2, PAIRS, ROWS * E)
    query_t = np.ascontiguousarray(query.reshape(B // 2, 2 * E).T).reshape(128, GROUPS * OCTETS, PAIRS)
    query_n = np.ascontiguousarray(
        query.reshape(GROUPS, OCTETS, PAIRS, 2, E).transpose(0, 2, 1, 3, 4)).reshape(GROUPS, PAIRS, ROWS, E)
    lengths = np.ascontiguousarray(
        length.reshape(GROUPS, OCTETS, PAIRS, 2).transpose(2, 1, 3, 0)).reshape(PAIRS, ROWS, GROUPS)

    weights = np.zeros((128, WEIGHTS), np.float32)
    for s in range(2):
        rows = slice(E * s, E * (s + 1))
        for n in range(4):
            at = W1_AT + n * WCOLS
            weights[rows, at + HEAD * s:at + HEAD * (s + 1)] = W1[E * n:E * (n + 1), :HEAD]
            tail = at + 2 * HEAD + TAIL * s
            weights[rows, tail:tail + TAIL] = W1[E * n:E * (n + 1), HEAD:]
        at = W2_AT + 64 * s
        weights[0:HEAD, at:at + H2] = W2[:HEAD]
        weights[HEAD + TAIL * s:HEAD + TAIL * (s + 1), at:at + H2] = W2[HEAD:]
        for o in range(OCTETS):
            weights[64 * s:64 * s + H2, W3_AT + QUAD * o + 2 * o + s] = W3[:, 0]
        weights[rows, BIAS_AT] = b1[:HEAD]
        weights[64 * s:64 * s + H2, BIAS_AT + 2] = b2
    for n in range(2 * PAIRS):
        weights[TAIL * n:TAIL * (n + 1), BIAS_AT + 1] = b1[HEAD:]
    weights[:, BIAS_AT + 3] = b3[0]

    consts = np.zeros((128, CONSTS), np.float32)
    consts[:, IDENT_AT:IOTA_AT] = np.eye(128)
    consts[:, IOTA_AT:OWN_AT] = np.arange(T)
    for q in range(PAIRS):
        for r in range(ROWS):
            consts[QUAD * q + r, OWN_AT + E * r:OWN_AT + E * (r + 1)] = 1

    given = {"keys_t": keys_t, "keys_n": keys_n, "query_t": query_t, "query_n": query_n,
             "lengths": lengths, "weights": weights, "consts": consts}
    nc = bacc.Bacc("TRN2", target_bir_lowering=False, num_devices=1)
    dram = {n: nc.dram_tensor(n, a.shape, mybir.dt.from_np(a.dtype), kind="ExternalInput").ap()
            for n, a in given.items()}
    out = nc.dram_tensor("out", (GROUPS, PAIRS, ROWS, 2 * E), FP32, kind="ExternalOutput").ap()
    build(nc, *dram.values(), out)
    done = run_bass_kernel_spmd(nc, [given], core_ids=[0]).results[0]["out"]
    return np.asarray(done).reshape(GROUPS, PAIRS, OCTETS, 2, 2 * E).transpose(0, 2, 1, 3, 4).reshape(B, 2 * E)
```

```python
import concourse.bass as bass
from concourse import mybir
from contextlib import ExitStack

FP32 = mybir.dt.float32
INT32 = mybir.dt.int32
ALU = mybir.AluOpType
ACT = mybir.ActivationFunctionType
AXIS = mybir.AxisListType

B, T, E = 2048, 200, 64
H1, H2 = 80, 40
HEAD, TAIL = 64, H1 - 64
PAIRS, OCTETS = 4, 4
GROUPS = B // (2 * PAIRS * OCTETS)
HALF = T // 2
ROWS = 2 * OCTETS
QUAD = 32
K2 = HEAD + QUAD
WCOLS = 2 * HEAD + QUAD
BIASES = PAIRS + 1
MASKED = -2.0 ** 32

W1_AT, W2_AT = 0, 4 * WCOLS
W3_AT = W2_AT + 2 * 64
BIAS_AT = W3_AT + OCTETS * QUAD
WEIGHTS = BIAS_AT + 4
IDENT_AT, IOTA_AT = 0, 128
OWN_AT = IOTA_AT + T
CONSTS = OWN_AT + ROWS * E


def build(nc, keys_t, keys_n, query_t, query_n, lengths, weights, consts, out):
    ctx = ExitStack()
    with ctx:
        def sbuf(name, shape, dtype=FP32):
            return ctx.enter_context(nc.sbuf_tensor(name, shape, dtype))

        def psum(name):
            return ctx.enter_context(nc.psum_tensor(name, [128, 512], FP32))

        def sem(name):
            return ctx.enter_context(nc.semaphore(name))

        key_t = sbuf("key_t", [128, OCTETS, PAIRS, T])
        key_n = sbuf("key_n", [HALF, 2, PAIRS, ROWS * E])
        h1 = sbuf("h1", [K2, 2, PAIRS, 2, T])
        h2 = sbuf("h2", [128, 2, PAIRS, T])
        w = sbuf("w", [128, WEIGHTS])
        c = sbuf("c", [128, CONSTS])
        w_key = sbuf("w_key", [128, WCOLS])
        w_query = sbuf("w_query", [128, WCOLS])
        q_all = sbuf("q_all", [128, GROUPS * OCTETS, PAIRS])
        biases = sbuf("biases", [128, GROUPS * OCTETS, BIASES])
        own_bias = sbuf("own_bias", [128, OCTETS, BIASES])
        w_own = sbuf("w_own", [128, 2, PAIRS, WCOLS])
        w_scaled = sbuf("w_scaled", [128, PAIRS, WCOLS])
        len_i = sbuf("len_i", [128, GROUPS], INT32)
        len_f = sbuf("len_f", [128, GROUPS])
        valid = sbuf("valid", [128, T])
        penalty = sbuf("penalty", [128, T])
        kept = sbuf("kept", [128, T])
        score = sbuf("score", [128, T])
        top = sbuf("top", [128, 1])
        neg_top = sbuf("neg_top", [128, 1])
        prob = sbuf("prob", [128, T])
        total = sbuf("total", [128, 1])
        inv_total = sbuf("inv_total", [128, 1])
        prob_t = sbuf("prob_t", [HALF, 2, 128])
        pooled_all = sbuf("pooled_all", [128, ROWS, E])
        pooled = sbuf("pooled", [128, E])

        w1d = w[:, W1_AT + 3 * WCOLS:W1_AT + 4 * WCOLS]
        w2 = w[:, W2_AT:W3_AT].rearrange("p (s j) -> p s j", s=2)
        w3 = w[:, W3_AT:BIAS_AT].rearrange("p (o j) -> p o j", o=OCTETS)
        b1_head, b1_tail, b2_col, b3_col = (w[:, BIAS_AT + n:BIAS_AT + n + 1] for n in range(4))
        ident = c[:, IDENT_AT:IOTA_AT]
        iota = c[:, IOTA_AT:OWN_AT]
        own_block = c[:, OWN_AT:CONSTS]

        head_ps = [psum(f"head{n}") for n in range(2)]
        tail_ps = psum("tail")
        h2_ps = ctx.enter_context(nc.psum_tensor("h2_ps", [128, 2, 512], FP32))
        logit_ps = psum("logit")
        prob_t_ps = psum("prob_t_ps")
        out_ps = psum("out_ps")

        w1_in = sem("w1_in")
        weights_in = sem("weights_in")
        consts_in = sem("consts_in")
        query_in = sem("query_in")
        lengths_in = sem("lengths_in")
        lengths_clear = sem("lengths_clear")
        lengths_ready = sem("lengths_ready")
        w1_ready = sem("w1_ready")
        bias_done = sem("bias_done")
        biases_ready = sem("biases_ready")
        key_t_in = [sem(f"key_t_in{o}") for o in range(OCTETS)]
        key_n_in = sem("key_n_in")
        own_step = sem("own_step")
        mask_step = sem("mask_step")
        head_done = sem("head_done")
        tail_done = sem("tail_done")
        h1_act = sem("h1_act")
        h1_dve = sem("h1_dve")
        h2_done = sem("h2_done")
        h2_ready = sem("h2_ready")
        logit_done = sem("logit_done")
        soft_step = sem("soft_step")
        prob_ready = sem("prob_ready")
        prob_t_done = sem("prob_t_done")
        prob_t_ready = sem("prob_t_ready")
        out_done = sem("out_done")
        pool_step = sem("pool_step")
        inv_ready = sem("inv_ready")
        stored = sem("stored")

        SOFT, POOL, OWN, MASK = 4, 2, 3, 2

        def wait(eng, semaphore, value):
            if not isinstance(value, int) or value > 0:
                eng.wait_ge(semaphore, value)

        block = ctx.enter_context(nc.Block())


        @block.sync
        def _(sp):
            def load_key_t(g, o):
                sp.dma_start(key_t[:, o], keys_t[g]).then_inc(key_t_in[o], 16)

            def load_key_n(i):
                sp.dma_start(key_n[0:96], keys_n[i, 0:96]).then_inc(key_n_in, 16)
                sp.dma_start(key_n[96:HALF], keys_n[i, 96:HALF]).then_inc(key_n_in, 16)

            def store(i):
                sp.wait_ge(pool_step, POOL * (i + 1))
                for q in range(PAIRS):
                    sp.dma_start(out[i, q, :, 0:E], pooled[QUAD * q:QUAD * q + ROWS]).then_inc(stored, 16)

            sp.dma_start(w[:, 0:W2_AT], weights[:, 0:W2_AT]).then_inc(w1_in, 16)
            sp.dma_start(q_all[:], query_t).then_inc(query_in, 16)
            sp.dma_start(w[:, W2_AT:WEIGHTS], weights[:, W2_AT:WEIGHTS]).then_inc(weights_in, 16)
            load_key_t(0, 0)
            load_key_t(1, 1)
            sp.dma_start(c[:], consts).then_inc(consts_in, 16)
            sp.wait_ge(lengths_clear, 1)
            for q in range(PAIRS):
                sp.dma_start(len_i[QUAD * q:QUAD * q + ROWS], lengths[q]).then_inc(lengths_in, 16)
            for o in range(2, OCTETS):
                load_key_t(o, o)
            load_key_n(0)
            sp.dma_start(out[:, :, :, E:2 * E], query_n).then_inc(stored, 16)

            def body(i, first):
                for o in range(OCTETS):
                    sp.wait_ge(tail_done, 4 * i + o + 1)
                    load_key_t(4 * i + 4 + o, o)
                    if o == 0 and not first:
                        store(i - 2)
                if not first:
                    sp.wait_ge(out_done, i)
                    load_key_n(i)

            body(0, True)
            for o in range(OCTETS):
                sp.wait_ge(tail_done, 4 + o + 1)
                load_key_t(8 + o, o)
            sp.wait_ge(out_done, 1)
            load_key_n(1)
            with sp.Fori(2, GROUPS - 1) as i:
                body(i, False)
            store(GROUPS - 3)
            sp.wait_ge(out_done, GROUPS - 1)
            load_key_n(GROUPS - 1)
            store(GROUPS - 2)
            store(GROUPS - 1)
            sp.wait_ge(stored, 16 * (PAIRS * GROUPS + 1))

        @block.gpsimd
        def _(pool):
            nc.gpsimd.memset(len_i[:], 0).then_inc(lengths_clear, 1)
            pool.wait_ge(w1_in, 16)
            pool.wait_ge(query_in, 16)
            pool.wait_ge(w1_ready, 1)

            def octet_weights(g, o):
                shape = [128, PAIRS, WCOLS]
                wait(pool, own_step, OWN * g)
                nc.gpsimd.tensor_tensor(
                    w_scaled[:], w1d[:, None, :].broadcast_to(shape),
                    q_all[:, g, :, None].broadcast_to(shape), ALU.mult).then_inc(own_step, 1)
                pool.wait_ge(own_step, OWN * g + 1)
                wait(pool, tail_done, g - 1)
                nc.gpsimd.tensor_tensor(
                    w_own[:, o % 2], w_scaled[:], w_key[:, None, :].broadcast_to(shape),
                    ALU.add).then_inc(own_step, 1)

            def octet_biases(g, o):
                nc.gpsimd.tensor_copy(own_bias[:, o], biases[:, g]).then_inc(own_step, 1)

            def body(i, first):
                for o in range(OCTETS):
                    octet_weights(4 * i + o, o)
                    if first and o == 0:
                        pool.wait_ge(biases_ready, 3)
                    octet_biases(4 * i + o, o)

            body(0, True)
            pool.wait_ge(lengths_in, 16 * PAIRS)
            nc.gpsimd.tensor_copy(len_f[:], len_i[:]).then_inc(lengths_ready, 1)
            with pool.Fori(1, GROUPS) as i:
                body(i, False)

        @block.tensor
        def _(pe):
            pe.wait_ge(w1_ready, 2)
            pe.wait_ge(query_in, 16)
            half = GROUPS * OCTETS // 2
            for n in range(2):
                nc.tensor.matmul(h2_ps[:, n], w_query[:, 0:2 * HEAD],
                                 q_all[:, n * half:(n + 1) * half].rearrange("p g n -> p (g n)"),
                                 start=True, stop=True).then_inc(bias_done, 1)
            for p in range(PAIRS):
                last = nc.tensor.matmul(out_ps[QUAD * p:QUAD * (p + 1), 0:GROUPS * OCTETS],
                                        w_query[:, 2 * HEAD:WCOLS], q_all[:, :, p],
                                        start=True, stop=True)
            last.then_inc(bias_done, 1)

            def layer1_heads(i, g, o):
                pe.wait_ge(key_t_in[o], 16 * (i + 1))
                pe.wait_ge(own_step, OWN * g + 2)
                for n in range(2):
                    wait(pe, h1_act, 3 * (g - 1) + n + 1)
                    wait(pe, h1_dve, 3 * (g - 1) + n + 1)
                    for p in (2 * n, 2 * n + 1):
                        last = nc.tensor.matmul(head_ps[n][:, T * (p % 2):T * (p % 2 + 1)],
                                                w_own[:, o % 2, p, 0:2 * HEAD], key_t[:, o, p],
                                                start=True, stop=True)
                    last.then_inc(head_done, 1)

            def layer1_tails(g, o):
                wait(pe, h1_act, 3 * g)
                wait(pe, h1_dve, 3 * g)
                for p in range(PAIRS):
                    last = nc.tensor.matmul(tail_ps[QUAD * p:QUAD * (p + 1), 0:T],
                                            w_own[:, o % 2, p, 2 * HEAD:WCOLS], key_t[:, o, p],
                                            start=True, stop=True)
                last.then_inc(tail_done, 1)

            def layer2(g, o):
                wait(pe, h2_ready, g)
                for n in range(2):
                    for s in range(2):
                        last = nc.tensor.matmul(
                            h2_ps[64 * s:64 * (s + 1), n, 0:2 * T], w2[0:K2, s],
                            h1[:, o % 2, 2 * n:2 * n + 2, s], start=True, stop=True)
                last.then_inc(h2_done, 1)

            def layer3(i, g, o):
                pe.wait_ge(h2_ready, g + 1)
                if o == 0:
                    wait(pe, soft_step, SOFT * (i - 1) + 1)
                for p in range(PAIRS):
                    last = nc.tensor.matmul(logit_ps[QUAD * p:QUAD * (p + 1), 0:T], w3[:, o],
                                            h2[:, o % 2, p], start=o == 0, stop=o == OCTETS - 1)
                last.then_inc(logit_done, 1)

            def turn_probs(i):
                pe.wait_ge(prob_ready, i + 1)
                wait(pe, prob_t_ready, i)
                for n in range(2):
                    last = nc.tensor.transpose(prob_t_ps[0:HALF, 128 * n:128 * (n + 1)],
                                               prob[:, HALF * n:HALF * (n + 1)], ident)
                last.then_inc(prob_t_done, 1)

            def pool_keys(i):
                pe.wait_ge(prob_t_ready, i + 1)
                pe.wait_ge(key_n_in, 32 * (i + 1))
                wait(pe, pool_step, POOL * (i - 1) + 1)
                for n in range(2):
                    for q in range(PAIRS):
                        last = nc.tensor.matmul(out_ps[QUAD * q:QUAD * (q + 1), 0:ROWS * E],
                                                prob_t[:, n, QUAD * q:QUAD * (q + 1)], key_n[:, n, q],
                                                start=n == 0, stop=n == 1)
                last.then_inc(out_done, 1)

            def body(i, first):
                for o in range(OCTETS):
                    g = 4 * i + o
                    layer1_heads(i, g, o)
                    if o == 3 and not first:
                        turn_probs(i - 1)
                    layer1_tails(g, o)
                    if o >= 2 or not first:
                        j = i if o >= 2 else i - 1
                        layer3(j, g - 2, (o - 2) % 4)
                    if o >= 1 or not first:
                        layer2(g - 1, (o - 1) % 4)
                    if o == 3 and not first:
                        pool_keys(i - 1)

            body(0, True)
            body(1, False)
            with nc.Fori(2, GROUPS, engines=[mybir.EngineType.PE], hint_back_edge=True) as i:
                body(i, False)
            i, g = GROUPS - 1, 4 * GROUPS
            layer3(i, g - 2, 2)
            pe.wait_ge(h1_act, 3 * g)
            pe.wait_ge(h1_dve, 3 * g)
            layer2(g - 1, 3)
            layer3(i, g - 1, 3)
            turn_probs(i)
            pool_keys(i)

        @block.scalar
        def _(act):
            def heads_of_first(g, o):
                act.wait_ge(own_step, OWN * (g + 1))
                for p in range(PAIRS):
                    if p % 2 == 0:
                        act.wait_ge(head_done, 2 * g + p // 2 + 1)
                    last = nc.scalar.activation(
                        h1[0:HEAD, o % 2, p, 0], head_ps[p // 2][0:HEAD, T * (p % 2):T * (p % 2 + 1)],
                        ACT.Relu, bias=own_bias[0:HEAD, o, p:p + 1])
                    if p % 2:
                        last.then_inc(h1_act, 1)

            def tails(g, o):
                act.wait_ge(tail_done, g + 1)
                for p in (0, 1):
                    rows = slice(QUAD * p, QUAD * (p + 1))
                    last = nc.scalar.activation(
                        h1[HEAD:K2, o % 2, p],
                        tail_ps[rows, None, 0:T].broadcast_to([QUAD, 2, T]),
                        ACT.Relu, bias=own_bias[rows, o, PAIRS:BIASES])
                last.then_inc(h1_act, 1)

            def layer2_out(g, o):
                wait(act, logit_done, g - 1)
                act.wait_ge(h2_done, g + 1)
                nc.scalar.activation(h2[:, o % 2].rearrange("p (n a) t -> p n (a t)", n=2),
                                     h2_ps[:, :, 0:2 * T], ACT.Relu, bias=b2_col).then_inc(h2_ready, 1)

            def exponentials(i):
                act.wait_ge(soft_step, SOFT * (i + 1))
                wait(act, prob_t_done, i)
                wait(act, inv_ready, i)
                nc.scalar.activation(prob[:], score[:], ACT.Exp, bias=neg_top[:, 0:1],
                                     accum_out=total[:, 0:1]).then_inc(prob_ready, 1)

            def body(i, first):
                for o in range(OCTETS):
                    g = 4 * i + o
                    if o >= 2 or not first:
                        layer2_out(g - 2, (o - 2) % 4)
                    heads_of_first(g, o)
                    tails(g, o)
                    if o == 2 and not first:
                        exponentials(i - 1)

            act.wait_ge(weights_in, 16)
            body(0, True)
            body(1, False)
            with act.Fori(2, GROUPS) as i:
                body(i, False)
            layer2_out(4 * GROUPS - 2, 2)
            layer2_out(4 * GROUPS - 1, 3)
            exponentials(GROUPS - 1)

        @block.vector
        def _(dve):
            dve.wait_ge(w1_in, 16)

            def w1(n):
                return w[:, W1_AT + n * WCOLS:W1_AT + (n + 1) * WCOLS]

            nc.vector.tensor_tensor(w_key[:], w1(1), w1(2), ALU.subtract).then_inc(w1_ready, 1)
            nc.vector.tensor_tensor(w_query[:], w1(0), w1(2), ALU.add).then_inc(w1_ready, 1)
            dve.wait_ge(weights_in, 16)
            half = GROUPS * OCTETS // 2
            for n in range(2):
                dve.wait_ge(bias_done, n + 1)
                nc.vector.tensor_scalar(
                    biases[:, n * half:(n + 1) * half, 0:PAIRS],
                    h2_ps[:, n].rearrange("p (g n) -> p g n", n=PAIRS),
                    b1_head, None, ALU.add).then_inc(biases_ready, 1)
            dve.wait_ge(bias_done, 3)
            nc.vector.tensor_scalar(biases[:, :, PAIRS], out_ps[:, 0:GROUPS * OCTETS],
                                    b1_tail, None, ALU.add).then_inc(biases_ready, 1)

            def heads_of_second(g, o):
                wait(dve, h2_done, g - 1)
                dve.wait_ge(own_step, OWN * (g + 1))
                for p in range(PAIRS):
                    if p % 2 == 0:
                        dve.wait_ge(head_done, 2 * g + p // 2 + 1)
                    last = nc.vector.tensor_scalar(
                        h1[0:HEAD, o % 2, p, 1], head_ps[p // 2][HEAD:128, T * (p % 2):T * (p % 2 + 1)],
                        own_bias[HEAD:128, o, p:p + 1], 0.0, ALU.add, ALU.max)
                    if p % 2:
                        last.then_inc(h1_dve, 1)

            def tails(g, o):
                dve.wait_ge(tail_done, g + 1)
                for p in (2, 3):
                    rows = slice(QUAD * p, QUAD * (p + 1))
                    last = nc.vector.tensor_scalar(
                        h1[HEAD:K2, o % 2, p],
                        tail_ps[rows, None, 0:T].broadcast_to([QUAD, 2, T]),
                        own_bias[rows, o, PAIRS:BIASES], 0.0, ALU.add, ALU.max)
                last.then_inc(h1_dve, 1)

            def masked_scores(i):
                length = len_f[:, bass.ds(i, 1)]
                nc.vector.tensor_scalar(valid[:], iota, length, None, ALU.is_lt).then_inc(mask_step, 1)
                nc.vector.tensor_scalar(penalty[:], iota, length, MASKED,
                                        ALU.is_ge, ALU.mult).then_inc(mask_step, 1)
                dve.wait_ge(logit_done, 4 * (i + 1))
                dve.wait_ge(mask_step, MASK * (i + 1))
                wait(dve, prob_ready, i)
                nc.vector.scalar_tensor_tensor(kept[:], logit_ps[:, 0:T], b3_col, valid[:],
                                               ALU.add, ALU.mult).then_inc(soft_step, 1)
                dve.wait_ge(soft_step, SOFT * i + 1)
                nc.vector.tensor_tensor(score[:], kept[:], penalty[:], ALU.add).then_inc(soft_step, 1)
                dve.wait_ge(soft_step, SOFT * i + 2)
                nc.vector.reduce_max(top[:], score[:], AXIS.X).then_inc(soft_step, 1)
                dve.wait_ge(soft_step, SOFT * i + 3)
                nc.vector.tensor_scalar(neg_top[:], top[:], -1.0, None, ALU.mult).then_inc(soft_step, 1)

            def probs_to_sbuf(i):
                dve.wait_ge(prob_t_done, i + 1)
                wait(dve, out_done, i)
                nc.vector.reciprocal(inv_total[:], total[:]).then_inc(inv_ready, 1)
                nc.vector.tensor_copy(prob_t[:].rearrange("p h n -> p (h n)"),
                                      prob_t_ps[0:HALF, 0:256]).then_inc(prob_t_ready, 1)

            def pooled_out(i):
                dve.wait_ge(out_done, i + 1)
                dve.wait_ge(inv_ready, i + 1)
                nc.vector.scalar_tensor_tensor(
                    pooled_all[:].rearrange("p r e -> p (r e)"), out_ps[:, :], inv_total[:, 0:1],
                    own_block, ALU.mult, ALU.mult).then_inc(pool_step, 1)
                dve.wait_ge(pool_step, POOL * i + 1)
                dve.wait_ge(stored, 16 * (PAIRS * i + 1))
                nc.vector.reduce_sum(pooled[:], pooled_all[:].rearrange("p r e -> p e r"),
                                     AXIS.X).then_inc(pool_step, 1)

            def body(i, first, second=False):
                for o in range(OCTETS):
                    g = 4 * i + o
                    heads_of_second(g, o)
                    if o == 3 and not first:
                        probs_to_sbuf(i - 1)
                    tails(g, o)
                    if o == 0 and not first and not second:
                        pooled_out(i - 2)
                    if o == 1 and not first:
                        masked_scores(i - 1)

            body(0, True)
            dve.wait_ge(lengths_ready, 1)
            dve.wait_ge(consts_in, 16)
            body(1, False, True)
            with dve.Fori(2, GROUPS) as i:
                body(i, False)
            pooled_out(GROUPS - 2)
            masked_scores(GROUPS - 1)
            probs_to_sbuf(GROUPS - 1)
            pooled_out(GROUPS - 1)


def kernel(r_query, r_keys, r_seq_len, L0_rec_W1, L0_rec_b1, L0_rec_W2, L0_rec_b2, L0_rec_W3, L0_rec_b3):
    import numpy as np
    import concourse.bacc as bacc
    from concourse.bass_utils import run_bass_kernel_spmd

    arrays = [np.asarray(x) for x in (r_query, r_keys, r_seq_len, L0_rec_W1, L0_rec_b1,
                                      L0_rec_W2, L0_rec_b2, L0_rec_W3, L0_rec_b3)]
    query, keys, length, W1, b1, W2, b2, W3, b3 = arrays

    keys_t = np.ascontiguousarray(
        keys.reshape(GROUPS * OCTETS, PAIRS, 2, T, E).transpose(0, 2, 4, 1, 3)
    ).reshape(GROUPS * OCTETS, 2 * E, PAIRS, T)
    keys_n = np.ascontiguousarray(
        keys.reshape(GROUPS, OCTETS, PAIRS, 2, 2, HALF, E).transpose(0, 5, 4, 2, 1, 3, 6)
    ).reshape(GROUPS, HALF, 2, PAIRS, ROWS * E)
    query_t = np.ascontiguousarray(query.reshape(B // 2, 2 * E).T).reshape(128, GROUPS * OCTETS, PAIRS)
    query_n = np.ascontiguousarray(
        query.reshape(GROUPS, OCTETS, PAIRS, 2, E).transpose(0, 2, 1, 3, 4)).reshape(GROUPS, PAIRS, ROWS, E)
    lengths = np.ascontiguousarray(
        length.reshape(GROUPS, OCTETS, PAIRS, 2).transpose(2, 1, 3, 0)).reshape(PAIRS, ROWS, GROUPS)

    weights = np.zeros((128, WEIGHTS), np.float32)
    for s in range(2):
        rows = slice(E * s, E * (s + 1))
        for n in range(4):
            at = W1_AT + n * WCOLS
            weights[rows, at + HEAD * s:at + HEAD * (s + 1)] = W1[E * n:E * (n + 1), :HEAD]
            tail = at + 2 * HEAD + TAIL * s
            weights[rows, tail:tail + TAIL] = W1[E * n:E * (n + 1), HEAD:]
        at = W2_AT + 64 * s
        weights[0:HEAD, at:at + H2] = W2[:HEAD]
        weights[HEAD + TAIL * s:HEAD + TAIL * (s + 1), at:at + H2] = W2[HEAD:]
        for o in range(OCTETS):
            weights[64 * s:64 * s + H2, W3_AT + QUAD * o + 2 * o + s] = W3[:, 0]
        weights[rows, BIAS_AT] = b1[:HEAD]
        weights[64 * s:64 * s + H2, BIAS_AT + 2] = b2
    for n in range(2 * PAIRS):
        weights[TAIL * n:TAIL * (n + 1), BIAS_AT + 1] = b1[HEAD:]
    weights[:, BIAS_AT + 3] = b3[0]

    consts = np.zeros((128, CONSTS), np.float32)
    consts[:, IDENT_AT:IOTA_AT] = np.eye(128)
    consts[:, IOTA_AT:OWN_AT] = np.arange(T)
    for q in range(PAIRS):
        for r in range(ROWS):
            consts[QUAD * q + r, OWN_AT + E * r:OWN_AT + E * (r + 1)] = 1

    given = {"keys_t": keys_t, "keys_n": keys_n, "query_t": query_t, "query_n": query_n,
             "lengths": lengths, "weights": weights, "consts": consts}
    nc = bacc.Bacc("TRN2", target_bir_lowering=False, num_devices=1)
    dram = {n: nc.dram_tensor(n, a.shape, mybir.dt.from_np(a.dtype), kind="ExternalInput").ap()
            for n, a in given.items()}
    out = nc.dram_tensor("out", (GROUPS, PAIRS, ROWS, 2 * E), FP32, kind="ExternalOutput").ap()
    build(nc, *dram.values(), out)
    done = run_bass_kernel_spmd(nc, [given], core_ids=[0]).results[0]["out"]
    return np.asarray(done).reshape(GROUPS, PAIRS, OCTETS, 2, 2 * E).transpose(0, 2, 1, 3, 4).reshape(B, 2 * E)
```
